# Optimizing a Trainium2 kernel written in Bass

```python
import numpy as np
import jax
import jax.numpy as jnp

def _softmax(x, axis=-1):
    return jax.nn.softmax(x, axis=axis)

def _gelu(x):
    return jax.nn.gelu(x, approximate=True)

def _silu(x):
    return jax.nn.silu(x)

def _sigmoid(x):
    return jax.nn.sigmoid(x)

def _layernorm(x, axis=-1, eps=1e-05):
    m = jnp.mean(x, axis=axis, keepdims=True)
    v = jnp.var(x, axis=axis, keepdims=True)
    return (x - m) / jnp.sqrt(v + eps)

def _scatter_add(tgt, idx, src, axis=0):
    return tgt.at[idx].add(src)

def _segment_sum(src, seg, n):
    return jax.ops.segment_sum(src, seg, n)
kernel_name = 'mk_gnn_preln_d2_gnn_r8_eaf36a'

def setup_inputs(seed: int=0):
    np.random.seed(seed)
    _w = jnp.asarray

    def _rec_inputs():
        import jax
        import jax.numpy as jnp
        _gk = jax.random.key(seed)
        x = -0.000202 + 1 * jax.random.normal(jax.random.fold_in(_gk, 1), (6250, 128), jnp.float32)
        src = jax.random.randint(jax.random.fold_in(_gk, 2), (200000,), 0, 6250, jnp.int32)
        dst = jnp.minimum((6250 * jax.random.uniform(jax.random.fold_in(_gk, 3), (200000,)) ** 2.0).astype(jnp.int32), 49999)
        _o = jnp.argsort(dst, stable=True)
        src = src[_o]
        dst = dst[_o]
        edge_attr_128 = -8.16379e-05 + 0.999858 * jax.random.normal(jax.random.fold_in(_gk, 12), (200000, 128), jnp.float32)
        return (x, src, dst, edge_attr_128)
    x, src, dst, edge_attr_128 = _rec_inputs()

    def _L0_gnn_setup():
        import jax, jax.numpy as jnp
        import numpy as np
        N_NODES = 6250
        N_EDGES = 100000
        NODE_DIM = 128
        EDGE_DIM = 128
        OUT_FEATS = 128
        key = jax.random.key(seed)
        k1, k2, k3, k4, k5, k6 = jax.random.split(key, 6)
        node_features = jax.random.normal(k1, (N_NODES, NODE_DIM), dtype=jnp.float32)
        edge_features = jax.random.normal(k2, (N_EDGES, EDGE_DIM), dtype=jnp.float32)
        src = jax.random.randint(k3, (N_EDGES,), 0, N_NODES, dtype=jnp.int32)
        dst = jax.random.randint(k4, (N_EDGES,), 0, N_NODES, dtype=jnp.int32)
        in_dim = 2 * NODE_DIM + EDGE_DIM
        W = jax.random.normal(k5, (OUT_FEATS, in_dim), dtype=jnp.float32) / np.sqrt(in_dim)
        b = jax.random.normal(k6, (OUT_FEATS,), dtype=jnp.float32) * 0.01
        return {'node_features': node_features, 'edge_features': edge_features, 'src': src, 'dst': dst, 'W': W, 'b': b}
    _L0_gnn_all = _L0_gnn_setup()
    _L0_gnn_in = {k: v for k, v in _L0_gnn_all.items() if k in ('W', 'b')}
    del _L0_gnn_all

    def _L1_gnn_setup():
        import jax, jax.numpy as jnp
        import numpy as np
        N = 6250
        F_IN = 128
        HID = 128
        E = 75000

        def _sage_conv(x_src, x_dst, src, dst, n_dst, W_l, b_l, W_r):
            msgs = x_src[src]
            agg = jax.ops.segment_sum(msgs, dst, num_segments=n_dst)
            deg = jax.ops.segment_sum(jnp.ones((src.shape[0],), x_src.dtype), dst, num_segments=n_dst)
            agg = agg / jnp.maximum(deg, 1.0)[:, None]
            return agg @ W_l + b_l + x_dst @ W_r
        key = jax.random.key(seed)
        k = jax.random.split(key, 8)
        s1 = 1.0 / np.sqrt(F_IN)
        s2 = 1.0 / np.sqrt(HID)
        return {'x': jax.random.normal(k[0], (N, F_IN), jnp.float32), 'edge_index': jax.random.randint(k[1], (2, E), 0, N, jnp.int64), 'W1_l': jax.random.uniform(k[2], (F_IN, HID), jnp.float32, -s1, s1), 'b1': jnp.zeros((HID,), jnp.float32), 'W1_r': jax.random.uniform(k[3], (F_IN, HID), jnp.float32, -s1, s1), 'W2_l': jax.random.uniform(k[4], (HID, F_IN), jnp.float32, -s2, s2), 'b2': jnp.zeros((F_IN,), jnp.float32), 'W2_r': jax.random.uniform(k[5], (HID, F_IN), jnp.float32, -s2, s2)}
    _L1_gnn_all = _L1_gnn_setup()
    _L1_gnn_in = {k: v for k, v in _L1_gnn_all.items() if k in ('W1_l', 'b1', 'W1_r', 'W2_l', 'b2', 'W2_r')}
    del _L1_gnn_all
    return {'x': x, 'src': src, 'dst': dst, 'edge_attr_128': edge_attr_128, 'L0_gnn_W': _L0_gnn_in['W'], 'L0_gnn_b': _L0_gnn_in['b'], 'L1_gnn_W1_l': _L1_gnn_in['W1_l'], 'L1_gnn_b1': _L1_gnn_in['b1'], 'L1_gnn_W1_r': _L1_gnn_in['W1_r'], 'L1_gnn_W2_l': _L1_gnn_in['W2_l'], 'L1_gnn_b2': _L1_gnn_in['b2'], 'L1_gnn_W2_r': _L1_gnn_in['W2_r']}

def reference(x, src, dst, edge_attr_128, L0_gnn_W, L0_gnn_b, L1_gnn_W1_l, L1_gnn_b1, L1_gnn_W1_r, L1_gnn_W2_l, L1_gnn_b2, L1_gnn_W2_r):
    import jax
    import jax.numpy as jnp

    def _L0_gnn_ref(node_features, edge_features, src, dst, W, b):
        import jax, jax.numpy as jnp
        import numpy as np
        N_NODES = 6250
        N_EDGES = 100000
        NODE_DIM = 128
        EDGE_DIM = 128
        OUT_FEATS = 128
        agg_src = jax.ops.segment_sum(node_features[src], dst, num_segments=N_NODES)
        agg_edge = jax.ops.segment_sum(edge_features, dst, num_segments=N_NODES)
        h = jnp.concatenate([node_features, agg_src, agg_edge], axis=1)
        h = h @ W.T + b
        return jax.nn.relu(h)

    def _L1_gnn_ref(x, edge_index, W1_l, b1, W1_r, W2_l, b2, W2_r):
        import jax, jax.numpy as jnp
        import numpy as np
        N = 6250
        F_IN = 128
        HID = 128
        E = 75000

        def _sage_conv(x_src, x_dst, src, dst, n_dst, W_l, b_l, W_r):
            msgs = x_src[src]
            agg = jax.ops.segment_sum(msgs, dst, num_segments=n_dst)
            deg = jax.ops.segment_sum(jnp.ones((src.shape[0],), x_src.dtype), dst, num_segments=n_dst)
            agg = agg / jnp.maximum(deg, 1.0)[:, None]
            return agg @ W_l + b_l + x_dst @ W_r
        src, dst = (edge_index[0], edge_index[1])
        h = jax.nn.relu(_sage_conv(x, x, src, dst, x.shape[0], W1_l, b1, W1_r))
        out = jax.nn.relu(_sage_conv(h, h, src, dst, x.shape[0], W2_l, b2, W2_r))
        return out
    edge_index = jnp.stack([src, dst])
    h = jnp.maximum(_layernorm(x, axis=-1), 0.0)
    x = x + _L0_gnn_ref(h, edge_attr_128, src, dst, L0_gnn_W, L0_gnn_b)
    h = jnp.maximum(_layernorm(x, axis=-1), 0.0)
    x = x + _L1_gnn_ref(h, edge_index, L1_gnn_W1_l, L1_gnn_b1, L1_gnn_W1_r, L1_gnn_W2_l, L1_gnn_b2, L1_gnn_W2_r)
    return x

_drawn_inputs = setup_inputs


def setup_inputs(seed=0):
    import zlib

    import numpy as np

    out = dict(_drawn_inputs(seed))
    spreads = {'L1_gnn_b1': (0.0, 0.8), 'L1_gnn_b2': (0.0, 0.8)}
    factors = {'L0_gnn_b': 64.0,
     'L1_gnn_W1_l': 4.22,
     'L1_gnn_W1_r': 3.645,
     'L1_gnn_W2_l': 3.973,
     'L1_gnn_W2_r': 3.111}
    for name, (base, spread) in spreads.items():
        noise = np.random.default_rng([zlib.crc32(name.encode()), seed]).standard_normal(out[name].shape)
        drawn = base * np.exp(spread * noise) if base else spread * noise
        out[name] = jnp.asarray(drawn.astype(out[name].dtype))
    for name, factor in factors.items():
        out[name] = (out[name] * factor).astype(out[name].dtype)
    return out
```

```python
from contextlib import ExitStack

import concourse.bass as bass
from concourse import mybir

P = 128
TILES = 4
GROUP = P * TILES
UNROLL = 4
CHUNK = 7

ALU = mybir.AluOpType
ACT = mybir.ActivationFunctionType
F32 = mybir.dt.float32
I32 = mybir.dt.int32
AX_X = mybir.AxisListType.X
EPS = 1e-5


def message_passing(nc, x, src, dst, edge_attr, L0_W, L0_b, W1_l, b1, W1_r, W2_l, b2, W2_r, out):
    N, D = x.shape
    E = src.shape[0]
    BLOCKS = -(-N // P)
    NPAD = BLOCKS * P
    TAIL = N - (BLOCKS - 1) * P
    GROUPS = -(-E // GROUP)
    LAST_ROW = E - GROUP
    SKIP = GROUPS * GROUP - E
    ROW_BLOCKS = -(-(GROUPS + 1) // P)
    WHOLE = (GROUPS - 1) // P
    REST = GROUPS - 1 - WHOLE * P
    STEPS = -(-(GROUPS + BLOCKS - 1) // UNROLL) * UNROLL
    GPAD = -(-GROUPS // UNROLL) * UNROLL
    assert D == P and BLOCKS % CHUNK == 0 and SKIP % TILES == 0 and GPAD == GROUPS + 1
    assert STEPS <= 512 and GROUPS - 1 <= 512

    with ExitStack() as ctx:
        def sb(name, shape, dt=F32):
            return ctx.enter_context(nc.sbuf_tensor(name, shape, dt))

        def sem(name):
            return ctx.enter_context(nc.semaphore(name))

        h_table = nc.dram_tensor("h_table", [NPAD, D], F32).ap()
        h_rows = h_table.rearrange("(b p) f -> p b f", p=P)

        x_sb = sb("x_sb", [P, BLOCKS, D])
        hT = sb("hT", [P, NPAD])
        agg_src = sb("agg_src", [P, NPAD])
        agg_edge = sb("agg_edge", [P, NPAD])
        degree = sb("degree", [P, NPAD])
        scratch = sb("scratch", [P, NPAD])
        hN = scratch[:, 0:NPAD].rearrange("p (b f) -> p b f", f=D)
        dst_col = sb("dst_col", [P, GPAD, TILES])
        src_col = sb("src_col", [P, GPAD, TILES], I32)
        edge_rows = sb("edge_rows", [P, UNROLL, TILES, D])
        src_rows = sb("src_rows", [P, UNROLL, TILES, D])
        src_idx = sb("src_idx", [P, UNROLL, TILES], I32)
        onehot = sb("onehot", [P, UNROLL, TILES, P])
        ident = sb("ident", [P, P])
        last_row_sel = sb("last_row_sel", [P, P])
        ones = sb("ones", [P, P])
        iota = sb("iota", [P, 512])
        part = sb("part", [P, 1])
        part_i = sb("part_i", [P, 1], I32)
        minus_base = sb("minus_base", [P, BLOCKS])
        w_in = agg_src[:, NPAD - 3 * D:NPAD].rearrange("o (k f) -> o k f", k=3)
        w_l0 = sb("w_l0", [P, 3, D])
        w_conv = sb("w_conv", [P, 4, D])
        bias = sb("bias", [1, 3, D])
        stats = sb("stats", [P, BLOCKS, 6])
        mean_var = sb("mean_var", [P, BLOCKS, 2])
        std = sb("std", [P, BLOCKS])
        scale = sb("scale", [P, BLOCKS])
        shift = sb("shift", [P, BLOCKS])
        eps = sb("eps", [P, 1])
        cmp = sb("cmp", [P, 512])
        iota_i = cmp[:, :].bitcast(I32)
        col = sb("col", [P, 4])
        tabf = degree[0:1, 0:4 * 512].rearrange("p (k f) -> p k f", f=4)
        table = sb("table", [1, 512, 4], I32)
        gtab = sb("gtab", [1, 512], I32)
        flag = sb("flag", [1, 1], I32)

        ps_step = [ctx.enter_context(nc.psum_tensor(f"ps_step{i}", [P, 4, D], F32)) for i in range(2)]
        ps_blk = [ctx.enter_context(nc.psum_tensor(f"ps_blk{i}", [P, 4, D], F32)) for i in range(4)]
        ps_turn = [ctx.enter_context(nc.psum_tensor(f"ps_turn{i}", [P, D], F32)) for i in range(2)]

        s_ready_copy = sem("s_ready_copy"); v_cmp = sem("v_cmp"); s_in = sem("s_in"); s_fill = sem("s_fill"); s_zero = sem("s_zero"); s_load = sem("s_load")
        v_done = sem("v_done"); p_done = sem("p_done"); s_ready = sem("s_ready")

        block = ctx.enter_context(nc.Block())

        RB = ROW_BLOCKS * GROUP
        row_views = [scratch[:, i * RB:(i + 1) * RB] for i in range(3)] + [agg_edge[:, 0:RB]]
        dst_rows, nxt_rows, srcs_rows = (v.bitcast(I32).rearrange("p (b e) -> p b e", e=GROUP) for v in row_views[:3])
        dst_f, src_f = row_views[3].rearrange("p (b e) -> p b e", e=GROUP), hT[:, 0:RB].rearrange("p (b e) -> p b e", e=GROUP)
        nxt_f = agg_src[:, 0:RB].rearrange("p (b e) -> p b e", e=GROUP)
        n_loads = [0]

        class Path:
            def __init__(self, kind):
                self.kind = kind
                self.iters = STEPS // UNROLL if kind == "sorted" else BLOCKS * (GPAD // UNROLL)
                self.total = self.iters * UNROLL
                n = lambda s: sem(f"{s}_{kind}")
                self.slot_free = n("slot_free")
                self.edge_landed = [n(f"edge_landed{u}") for u in range(UNROLL)]
                self.src_landed = [n(f"src_landed{u}") for u in range(UNROLL)]
                self.idx_ready = n("idx_ready")
                self.idx_seen = n("idx_seen")
                self.onehot_ready = n("onehot_ready")
                self.acc_done = n("acc_done")
                self.stats_done = n("stats_done")
                self.std_done = n("std_done")
                self.norm_done = n("norm_done")
                self.h_done = n("h_done")
                self.turned = n("turned")
                self.hT_done = n("hT_done")
                self.table_written = n("table_written")
                self.zeroed = n("zeroed")
                self.agg_final = n("agg_final")
                self.dense_done = n("dense_done")
                self.mixed = n("mixed")
                self.out_written = n("out_written")
                self.dve = n("dve")

        fast, slow = Path("sorted"), Path("any")

        def steps(eng, path, want):
            if path.kind == "sorted":
                with eng.Fori(0, path.iters) as it:
                    def field(u, f, top):
                        return eng.value_load(table[0:1, bass.ds(it * UNROLL + u, 1), f], min_val=0, max_val=top)
                    yield it, [{f: field(u, *{"col": (0, NPAD - P), "g": (1, GPAD - 1), "row": (2, LAST_ROW), "w": (3, BLOCKS - 1)}[f])
                                for f in want} for u in range(UNROLL)]
            else:
                with eng.Fori(0, BLOCKS) as w:
                    with eng.Fori(0, GPAD // UNROLL) as q:
                        it = eng.snap(w * (GPAD // UNROLL) + q)
                        out_ = []
                        for u in range(UNROLL):
                            d = {"w": w, "g": q * UNROLL + u, "col": w * P}
                            if "row" in want:
                                d["row"] = eng.value_load(gtab[0:1, bass.ds(q * UNROLL + u, 1)], min_val=0, max_val=LAST_ROW)
                            out_.append(d)
                        yield it, out_

        @block.sync
        def _(sp):
            def load(o, i):
                sp.dma_start(o, i).then_inc(s_load, 16)
                n_loads[0] += 1
            sp.wait_ge(s_fill, 1)
            W = WHOLE * P * GROUP
            R = W + REST * GROUP
            for rows, a in ((dst_rows, dst), (srcs_rows, src)):
                load(rows[:, 0:WHOLE, :], a[0:W].rearrange("(b p e) -> p b e", p=P, e=GROUP))
                load(rows[0:REST, WHOLE, :], a[W:R].rearrange("(p e) -> p e", e=GROUP))
                load(rows[REST:REST + 1, WHOLE, SKIP:GROUP], a[R:E].rearrange("(p e) -> p e", p=1))
            load(nxt_rows[:, 0:WHOLE, :], dst[1:W + 1].rearrange("(b p e) -> p b e", p=P, e=GROUP))
            load(nxt_rows[0:REST, WHOLE, :], dst[W + 1:R + 1].rearrange("(p e) -> p e", e=GROUP))
            load(nxt_rows[REST:REST + 1, WHOLE, SKIP:GROUP - 1], dst[R + 1:E].rearrange("(p e) -> p e", p=1))
            load(x_sb[:, 0:BLOCKS - 1, :], x[0:(BLOCKS - 1) * P].rearrange("(b p) f -> p b f", p=P))
            load(x_sb[0:TAIL, BLOCKS - 1, :], x[(BLOCKS - 1) * P:N])
            load(w_in[:, :, :], L0_W.rearrange("o (k f) -> o k f", k=3))
            for i, w in enumerate((W1_l, W1_r, W2_l, W2_r)):
                load(w_conv[:, i, :], w)
            for i, b in enumerate((L0_b, b1, b2)):
                load(bias[:, i, :], b.rearrange("(a o) -> a o", a=1))

            sp.wait_ge(s_ready, 1)
            go = sp.value_load(flag[0:1, 0:1], min_val=0, max_val=1)

            def run(path):
                for r in range(3):
                    for c in range(BLOCKS // CHUNK):
                        sp.wait_ge(path.h_done, (r * (BLOCKS // CHUNK) + c + 1))
                        sp.dma_start(h_rows[:, c * CHUNK:(c + 1) * CHUNK, :],
                                     hN[:, c * CHUNK:(c + 1) * CHUNK, :]).then_inc(path.table_written, 16)
                    if r == 0:
                        for it, st in steps(sp, path, ["row"]):
                            for u in range(UNROLL):
                                sp.wait_ge(path.slot_free, it * UNROLL + u + 1)
                                sp.dma_start(edge_rows[:, u, :, :],
                                             edge_attr[bass.ds(st[u]["row"], GROUP), :].rearrange("(p j) f -> p j f", j=TILES)
                                             ).then_inc(path.edge_landed[u], 16)
                sp.wait_ge(path.mixed, 3 * BLOCKS)
                sp.dma_start(out[0:(BLOCKS - 1) * P].rearrange("(b p) f -> p b f", p=P),
                             x_sb[:, 0:BLOCKS - 1, :]).then_inc(path.out_written, 16)
                sp.dma_start(out[(BLOCKS - 1) * P:N], x_sb[0:TAIL, BLOCKS - 1, :]).then_inc(path.out_written, 16)
                sp.wait_ge(path.out_written, 32)

            with sp.If(go > 0):
                run(fast)
            with sp.Else():
                run(slow)

        @block.gpsimd
        def _(pool):
            pool.memset(scratch[:, 0:RB].bitcast(I32), -1)
            pool.memset(scratch[:, RB:2 * RB].bitcast(I32), NPAD * 2)
            pool.memset(scratch[:, 2 * RB:3 * RB].bitcast(I32), 0)
            pool.memset(x_sb[:, BLOCKS - 1, :], 0.0)
            pool.memset(ident[:, :], 0.0)
            pool.memset(last_row_sel[:, :], 0.0)
            pool.memset(eps[:, :], EPS)
            pool.memset(ones[:, :], 1.0).then_inc(s_zero, 1)
            pool.wait_ge(s_zero, 1)
            pool.sem_inc(s_fill, 1)
            pool.affine_select(out=ident[:, :], in_=ident[:, :], compare_op=ALU.not_equal, fill=1.0, base=0,
                               pattern=[[-1, P]], channel_multiplier=1)
            pool.affine_select(out=last_row_sel[:, :], in_=last_row_sel[:, :], compare_op=ALU.not_equal, fill=1.0,
                               base=-(P - 1), pattern=[[0, P]], channel_multiplier=1)
            pool.iota(iota_i[:, :], [[1, 512]], base=0, channel_multiplier=0)
            pool.iota(part_i[:, :], [[1, 1]], base=0, channel_multiplier=1).then_inc(s_in, 1)
            pool.wait_ge(s_ready, 1)
            go = pool.value_load(flag[0:1, 0:1], min_val=0, max_val=1)

            def run(path):
                for r in range(3):
                    pool.wait_ge(path.table_written, 16 * (BLOCKS // CHUNK) * (r + 1))
                    for it, st in steps(pool, path, ["g"]):
                        for u in range(UNROLL):
                            k = it * UNROLL + u + r * path.total
                            pool.wait_ge(path.slot_free, k + 1)
                            pool.tensor_copy(src_idx[:, u, :], src_col[:, bass.ds(st[u]["g"], 1), :].rearrange("p a j -> p (a j)")
                                             ).then_inc(path.idx_ready, 1)
                            pool.wait_ge(path.idx_ready, k + 1)
                            pool.sem_inc(path.idx_seen, 1)
                            for j in range(TILES):
                                pool.indirect_dma_start(src_rows[:, u, j, :], None, h_table,
                                                        bass.IndirectOffsetOnAxis(ap=src_idx[:, u, j:j + 1], axis=0)
                                                        ).then_inc(path.src_landed[u], 16)
            with pool.If(go > 0):
                run(fast)
            with pool.Else():
                run(slow)

        @block.tensor
        def _(pe):
            n = 0
            for a, rows in enumerate((dst_f, src_f)):
                pe.wait_ge(v_done, [3, 4][a])
                for b in range(ROW_BLOCKS):
                    ps = ps_blk[n % 4]
                    if n >= 4:
                        pe.wait_ge(s_ready_copy, n - 3)
                    for j in range(TILES):
                        mm = pe.transpose(ps[:, j, :], rows[:, b, j::TILES], ident[:, :])
                    mm.then_inc(p_done, 1)
                    n += 1
            pe.wait_ge(s_ready_copy, n)
            for k in range(3):
                mm = pe.transpose(ps_blk[0][:, k, :], w_in[:, k, :], ident[:, :])
            mm.then_inc(p_done, 1)
            pe.matmul(ps_blk[1].ap().rearrange("p a b -> p (a b)")[:, 0:GROUPS - 1], last_row_sel[:, :], dst_col[:, 0:GROUPS - 1, TILES - 1],
                      start=True, stop=True).then_inc(p_done, 1)
            pe.wait_ge(v_cmp, 1)
            pe.matmul(ps_blk[2].ap().rearrange("p a b -> p (a b)")[:, 0:STEPS], ones[0:BLOCKS - 1, :], cmp[0:BLOCKS - 1, 0:STEPS],
                      start=True, stop=True).then_inc(p_done, 1)
            pe.wait_ge(v_cmp, 2)
            pe.matmul(ps_blk[3][:, 0, 0:1], ones[:, :], col[:, 3:4], start=True, stop=True).then_inc(p_done, 1)

            pe.wait_ge(s_ready, 1)
            go = pe.value_load(flag[0:1, 0:1], min_val=0, max_val=1)

            def run(path):
                pe.sem_inc(path.slot_free, UNROLL)
                for r in range(3):
                    for b in range(BLOCKS):
                        pe.wait_ge(path.norm_done, r * BLOCKS + b + 1)
                        g = r * BLOCKS + b
                        if g >= 2:
                            pe.wait_ge(path.hT_done, g - 1)
                        pe.transpose(ps_turn[g % 2][:, :], hN[:, b, :], ident[:, :]).then_inc(path.turned, 1)
                    for it, st in steps(pe, path, []):
                        for u in range(UNROLL):
                            k = it * UNROLL + u + r * path.total
                            ps = ps_step[u % 2]
                            pe.wait_ge(path.onehot_ready, k + 1)
                            pe.wait_ge(path.acc_done, k + 1)
                            if r == 0:
                                pe.wait_ge(path.edge_landed[u], it * 16 + 16)
                                for j in range(TILES):
                                    pe.matmul(ps[:, 1, :], edge_rows[:, u, j, :], onehot[:, u, j, :], start=j == 0, stop=j == TILES - 1)
                                for j in range(TILES):
                                    pe.matmul(ps[:, 2, :], ones[:, :], onehot[:, u, j, :], start=j == 0, stop=j == TILES - 1)
                            pe.wait_ge(path.src_landed[u], it * 64 + 64 + r * 64 * path.iters)
                            for j in range(TILES):
                                mm = pe.matmul(ps[:, 0, :], src_rows[:, u, j, :], onehot[:, u, j, :], start=j == 0, stop=j == TILES - 1)
                            mm.then_inc(path.slot_free, 1)
                    pe.wait_ge(path.agg_final, r + 1)
                    for b in range(BLOCKS):
                        g = r * BLOCKS + b
                        if g >= 4:
                            pe.wait_ge(path.mixed, g - 3)
                        ps = ps_blk[g % 4][:, 1, :]
                        at = slice(b * P, b * P + P)
                        if r == 0:
                            terms = [(hT, w_l0[:, 0, :]), (agg_src, w_l0[:, 1, :]), (agg_edge, w_l0[:, 2, :])]
                        else:
                            terms = [(agg_src, w_conv[:, 2 * r - 2, :]), (hT, w_conv[:, 2 * r - 1, :])]
                        pe.matmul(ps, ones[0:1, :], bias[0:1, r, :], start=True, stop=False)
                        for i, (a, w) in enumerate(terms):
                            mm = pe.matmul(ps, a[:, at], w, start=False, stop=i == len(terms) - 1)
                        mm.then_inc(path.dense_done, 1)
            with pe.If(go > 0):
                run(fast)
            with pe.Else():
                run(slow)

        @block.scalar
        def _(act):
            act.wait_ge(s_ready, 1)
            go = act.value_load(flag[0:1, 0:1], min_val=0, max_val=1)

            def run(path):
                for r in range(3):
                    if r > 0:
                        act.wait_ge(path.table_written, 16 * (BLOCKS // CHUNK) * r)
                    if r < 2:
                        act.wait_ge(path.stats_done, 2 * r + 1)
                        act.activation(std[:, :], mean_var[:, :, 1], ACT.Sqrt, bias=eps[:, 0:1]).then_inc(path.std_done, 1)
                        act.wait_ge(path.stats_done, 2 * r + 2)
                    for b in range(BLOCKS):
                        if r < 2:
                            mm = act.activation(hN[:, b, :], x_sb[:, b, :], ACT.Relu, bias=shift[:, b:b + 1], scale=scale[:, b:b + 1])
                            mm.then_inc(path.norm_done, 1)
                            if b % CHUNK == CHUNK - 1:
                                act.wait_ge(path.norm_done, r * BLOCKS + b + 1)
                                act.sem_inc(path.h_done, 1)
                        else:
                            act.wait_ge(path.dense_done, BLOCKS + b + 1)
                            act.activation(hN[:, b, :], ps_blk[(BLOCKS + b) % 4][:, 1, :], ACT.Relu).then_inc(path.norm_done, 1)
                            act.wait_ge(path.norm_done, r * BLOCKS + b + 1)
                            act.sem_inc(path.mixed, 1)
                            if b % CHUNK == CHUNK - 1:
                                act.sem_inc(path.h_done, 1)
                        g = r * BLOCKS + b
                    for b in range(BLOCKS):
                        g = r * BLOCKS + b
                        act.wait_ge(path.turned, g + 1)
                        act.activation(hT[:, b * P:(b + 1) * P], ps_turn[g % 2][:, :], ACT.Copy).then_inc(path.hT_done, 1)
            with act.If(go > 0):
                run(fast)
            with act.Else():
                run(slow)



        @block.vector
        def _(dve):
            cnt = [0]

            def link(ins):
                cnt[0] += 1
                ins.then_inc(v_done, 1)
                dve.wait_ge(v_done, cnt[0])

            dve.wait_ge(s_in, 1)
            link(dve.tensor_copy(iota[:, :], iota_i[:, :]))
            link(dve.tensor_copy(part[:, :], part_i[:, :]))
            dve.wait_ge(s_load, 16 * n_loads[0])
            link(dve.tensor_copy(row_views[3], row_views[0].bitcast(I32)))
            link(dve.tensor_copy(hT[:, 0:RB], row_views[2].bitcast(I32)))
            link(dve.tensor_copy(agg_src[:, 0:RB], row_views[1].bitcast(I32)))
            link(dve.tensor_scalar(minus_base[:, :], iota[:, 0:BLOCKS], -float(P), None, ALU.mult))
            n = 0
            for a, to in enumerate((dst_col, src_col)):
                for b in range(ROW_BLOCKS):
                    dve.wait_ge(p_done, n + 1)
                    w = min(P, GPAD - b * P)
                    dve.tensor_copy(to[:, b * P:b * P + w, :], ps_blk[n % 4][:, :, 0:w].rearrange("p j g -> p g j")).then_inc(s_ready_copy, 1)
                    n += 1
            dve.wait_ge(p_done, n + 1)
            link(dve.tensor_copy(w_l0[:, :, :], ps_blk[0][:, 0:3, :]))
            link(dve.tensor_scalar(col[:, 0:1], part[:, :], float(P), float(P), ALU.mult, ALU.add))
            dve.wait_ge(p_done, n + 2)
            link(dve.tensor_scalar(cmp[:, 0:GROUPS - 1], ps_blk[1].ap().rearrange("p a b -> p (a b)")[:, 0:GROUPS - 1], col[:, 0:1], None, ALU.is_lt))
            link(dve.tensor_reduce(col[:, 1:2], cmp[:, 0:GROUPS - 1], AX_X, ALU.add))
            link(dve.scalar_tensor_tensor(out=col[:, 2:3], in0=col[:, 1:2], scalar=1.0, in1=part[:, :], op0=ALU.add, op1=ALU.add))
            dve.tensor_scalar(cmp[:, 0:STEPS], iota[:, 0:STEPS], col[:, 2:3], None, ALU.is_ge).then_inc(v_cmp, 1)
            dve.wait_ge(p_done, n + 3)
            win = ps_blk[2].ap().rearrange("p a b -> p (a b)")[0:1, 0:STEPS]
            link(dve.tensor_scalar(tabf[:, 0:STEPS, 0], win, float(P), None, ALU.mult))
            link(dve.tensor_tensor(tabf[:, 0:STEPS, 1], iota[0:1, 0:STEPS], win, ALU.subtract))
            link(dve.tensor_scalar(tabf[:, 0:STEPS, 2], tabf[:, 0:STEPS, 1], float(GROUP), float(LAST_ROW), ALU.mult, ALU.min))
            link(dve.tensor_copy(tabf[:, 0:STEPS, 3], win))
            link(dve.tensor_copy(table[:, 0:STEPS, :], tabf[:, 0:STEPS, :]))
            link(dve.tensor_scalar(tabf[:, :, 0], iota[0:1, :], float(GROUP), float(LAST_ROW), ALU.mult, ALU.min))
            link(dve.tensor_copy(gtab[:, :], tabf[:, :, 0]))
            link(dve.tensor_tensor(dst_f, dst_f, nxt_f, ALU.is_gt))
            dve.tensor_reduce(col[:, 3:4], row_views[3], AX_X, ALU.max).then_inc(v_cmp, 1)
            dve.wait_ge(p_done, n + 4)
            link(dve.tensor_scalar(tabf[:, 0, 0:1], ps_blk[3][0:1, 0, 0:1], 0.0, None, ALU.is_equal))
            link(dve.tensor_copy(flag[:, :], tabf[:, 0, 0:1]))
            dve.sem_inc(s_ready, 1)
            go = dve.value_load(flag[0:1, 0:1], min_val=0, max_val=1)

            def run(path):
                c = [0]

                def chain(ins):
                    c[0] += 1
                    ins.then_inc(path.dve, 1)
                    dve.wait_ge(path.dve, c[0])

                dve.sem_inc(path.acc_done, 2)
                for r in range(3):
                    if r < 2:
                        for b in range(BLOCKS):
                            if r == 1:
                                dve.wait_ge(path.mixed, b + 1)
                            ins = dve.bn_stats(stats[:, b, :], x_sb[:, b, :])
                        chain(ins)
                        for b in range(BLOCKS):
                            ins = dve.bn_aggr(mean_var[:, b, :], stats[:, b, :])
                        chain(ins)
                        dve.sem_inc(path.stats_done, 1)
                        dve.wait_ge(path.std_done, r + 1)
                        chain(dve.reciprocal(scale[:, :], std[:, :]))
                        chain(dve.scalar_tensor_tensor(out=shift[:, :], in0=mean_var[:, :, 0], scalar=-1.0, in1=scale[:, :],
                                                       op0=ALU.mult, op1=ALU.mult))
                        dve.sem_inc(path.stats_done, 1)
                    if r > 0:
                        dve.wait_ge(path.dense_done, r * BLOCKS)
                    chain(dve.memset(agg_src[:, :], 0.0))
                    if r == 0:
                        chain(dve.memset(agg_edge[:, :], 0.0))
                        chain(dve.memset(degree[:, :], 0.0))

                    def take(u, it, col_):
                        k = it * UNROLL + u + r * path.total
                        dve.wait_ge(path.slot_free, k + 1 + UNROLL)
                        dve.wait_ge(path.acc_done, k + 2)
                        for i, acc in enumerate((agg_src, agg_edge, degree) if r == 0 else (agg_src,)):
                            a = acc[:, bass.ds(col_, P)]
                            ins = dve.tensor_tensor(a, a, ps_step[u % 2][:, i, :], ALU.add)
                        ins.then_inc(path.acc_done, 1)

                    for it, st in steps(dve, path, ["col", "g", "w"]):
                        for u in range(UNROLL):
                            k = it * UNROLL + u + r * path.total
                            dve.wait_ge(path.slot_free, k + 1)
                            for j in range(TILES):
                                d = dst_col[:, bass.ds(st[u]["g"], 1), j]
                                ins = dve.tensor_scalar(onehot[:, u, j, :], iota[:, 0:P], d, minus_base[:, bass.ds(st[u]["w"], 1)],
                                                        ALU.subtract, ALU.is_equal)
                            ins.then_inc(path.onehot_ready, 1)
                            if u > 0:
                                take(u - 1, it, st[u - 1]["col"])
                        take(UNROLL - 1, it, st[UNROLL - 1]["col"])
                    dve.wait_ge(path.acc_done, 2 + (r + 1) * path.total)
                    if r == 0:
                        chain(dve.tensor_scalar(degree[:, :], degree[:, :], 1.0, None, ALU.max))
                        chain(dve.reciprocal(degree[:, :], degree[:, :]))
                    else:
                        chain(dve.tensor_tensor(agg_src[:, :], agg_src[:, :], degree[:, :], ALU.mult))
                    dve.wait_ge(path.hT_done, (r + 1) * BLOCKS)
                    dve.sem_inc(path.agg_final, 1)
                    if r != 1:
                        for b in range(BLOCKS):
                            g = r * BLOCKS + b
                            dve.wait_ge(path.dense_done, g + 1)
                            dve.scalar_tensor_tensor(out=x_sb[:, b, :], in0=ps_blk[g % 4][:, 1, :], scalar=0.0, in1=x_sb[:, b, :],
                                                     op0=ALU.max, op1=ALU.add).then_inc(path.mixed, 1)
            with dve.If(go > 0):
                run(fast)
            with dve.Else():
                run(slow)


_INS = ['x', 'src', 'dst', 'edge_attr_128', 'L0_gnn_W', 'L0_gnn_b', 'L1_gnn_W1_l', 'L1_gnn_b1', 'L1_gnn_W1_r',
        'L1_gnn_W2_l', 'L1_gnn_b2', 'L1_gnn_W2_r']


def kernel(**inputs):
    import numpy as _np
    import concourse.bacc as _bacc
    from concourse import mybir as _mybir
    from concourse.bass_utils import run_bass_kernel_spmd as _run

    nc = _bacc.Bacc("TRN2", target_bir_lowering=False, num_devices=1)
    arrays, args = {}, []
    for name in _INS:
        a = _np.ascontiguousarray(inputs[name])
        arrays[f"in_{name}"] = a
        args.append(nc.dram_tensor(f"in_{name}", a.shape, _mybir.dt.from_np(a.dtype), kind="ExternalInput").ap())
    out = nc.dram_tensor("out", inputs['x'].shape, F32, kind="ExternalOutput").ap()
    message_passing(nc, *args, out)
    r = _run(nc, [arrays], core_ids=[0])
    return r.results[0]["out"]
```
